# Optimizing a Trainium2 kernel written in Bass

```python
import numpy as np
import jax
import jax.numpy as jnp

def _softmax(x, axis=-1):
    return jax.nn.softmax(x, axis=axis)

def _gelu(x):
    return jax.nn.gelu(x, approximate=True)

def _silu(x):
    return jax.nn.silu(x)

def _sigmoid(x):
    return jax.nn.sigmoid(x)

def _layernorm(x, axis=-1, eps=1e-05):
    m = jnp.mean(x, axis=axis, keepdims=True)
    v = jnp.var(x, axis=axis, keepdims=True)
    return (x - m) / jnp.sqrt(v + eps)

def _scatter_add(tgt, idx, src, axis=0):
    return tgt.at[idx].add(src)

def _segment_sum(src, seg, n):
    return jax.ops.segment_sum(src, seg, n)
kernel_name = 'mk_gnn_resnorm_d1_gnn_r16_770e80'

def setup_inputs(seed: int=0):
    np.random.seed(seed)
    _w = jnp.asarray

    def _rec_inputs():
        import jax
        import jax.numpy as jnp
        _gk = jax.random.key(seed)
        x = 7.22e-05 + 1 * jax.random.normal(jax.random.fold_in(_gk, 1), (4096, 128), jnp.float32)
        _s = jax.random.randint(jax.random.fold_in(_gk, 2), (65536,), 0, 4096, jnp.int32)
        _d = jax.random.randint(jax.random.fold_in(_gk, 3), (65536,), 0, 4096, jnp.int32)
        _loop = jnp.arange(4096, dtype=jnp.int32)
        src = jnp.concatenate([_s, _d, _loop])
        dst = jnp.concatenate([_d, _s, _loop])
        _o = jnp.argsort(dst, stable=True)
        src = src[_o]
        dst = dst[_o]
        edge_attr_64 = -1.52775e-05 + 0.999936 * jax.random.normal(jax.random.fold_in(_gk, 11), (135168, 64), jnp.float32)
        return (x, src, dst, edge_attr_64)
    x, src, dst, edge_attr_64 = _rec_inputs()

    def _L0_gnn_setup():
        import jax, jax.numpy as jnp
        import numpy as np
        NUM_NODES = 128
        N = 4096
        E = 32768
        D = 128
        ED = 64
        H = 256
        M = 128
        U = 256

        def _mlp3(x, W1, b1, W2, b2, W3, b3):
            h = jax.nn.relu(x @ W1 + b1)
            h = jax.nn.relu(h @ W2 + b2)
            return h @ W3 + b3
        key = jax.random.key(seed)
        ks = jax.random.split(key, 16)
        s = 0.02
        inp = {'node_states': jax.random.normal(ks[0], (N, D), jnp.float32), 'edges': jax.random.normal(ks[1], (E, ED), jnp.float32), 'vertices': jax.random.randint(ks[2], (E, 2), 0, N, jnp.int32), 'mW1': jax.random.normal(ks[3], (2 * D + ED, H), jnp.float32) * s, 'mb1': jnp.zeros((H,), jnp.float32), 'mW2': jax.random.normal(ks[4], (H, H), jnp.float32) * s, 'mb2': jnp.zeros((H,), jnp.float32), 'mW3': jax.random.normal(ks[5], (H, M), jnp.float32) * s, 'mb3': jnp.zeros((M,), jnp.float32), 'uW1': jax.random.normal(ks[6], (D + M + D, U), jnp.float32) * s, 'ub1': jnp.zeros((U,), jnp.float32), 'uW2': jax.random.normal(ks[7], (U, U), jnp.float32) * s, 'ub2': jnp.zeros((U,), jnp.float32), 'uW3': jax.random.normal(ks[8], (U, D), jnp.float32) * s, 'ub3': jnp.zeros((D,), jnp.float32)}
        return inp
    _L0_gnn_all = _L0_gnn_setup()
    _L0_gnn_in = {k: v for k, v in _L0_gnn_all.items() if k in ('mW1', 'mb1', 'mW2', 'mb2', 'mW3', 'mb3', 'uW1', 'ub1', 'uW2', 'ub2', 'uW3', 'ub3')}
    del _L0_gnn_all
    return {'x': x, 'src': src, 'dst': dst, 'edge_attr_64': edge_attr_64, 'L0_gnn_mW1': _L0_gnn_in['mW1'], 'L0_gnn_mb1': _L0_gnn_in['mb1'], 'L0_gnn_mW2': _L0_gnn_in['mW2'], 'L0_gnn_mb2': _L0_gnn_in['mb2'], 'L0_gnn_mW3': _L0_gnn_in['mW3'], 'L0_gnn_mb3': _L0_gnn_in['mb3'], 'L0_gnn_uW1': _L0_gnn_in['uW1'], 'L0_gnn_ub1': _L0_gnn_in['ub1'], 'L0_gnn_uW2': _L0_gnn_in['uW2'], 'L0_gnn_ub2': _L0_gnn_in['ub2'], 'L0_gnn_uW3': _L0_gnn_in['uW3'], 'L0_gnn_ub3': _L0_gnn_in['ub3']}

def reference(x, src, dst, edge_attr_64, L0_gnn_mW1, L0_gnn_mb1, L0_gnn_mW2, L0_gnn_mb2, L0_gnn_mW3, L0_gnn_mb3, L0_gnn_uW1, L0_gnn_ub1, L0_gnn_uW2, L0_gnn_ub2, L0_gnn_uW3, L0_gnn_ub3):
    import jax
    import jax.numpy as jnp

    def _L0_gnn_ref(node_states, edges, vertices, mW1, mb1, mW2, mb2, mW3, mb3, uW1, ub1, uW2, ub2, uW3, ub3):
        import jax, jax.numpy as jnp
        import numpy as np
        NUM_NODES = 128
        N = 4096
        E = 32768
        D = 128
        ED = 64
        H = 256
        M = 128
        U = 256

        def _mlp3(x, W1, b1, W2, b2, W3, b3):
            h = jax.nn.relu(x @ W1 + b1)
            h = jax.nn.relu(h @ W2 + b2)
            return h @ W3 + b3
        nodes_i = node_states[vertices[:, 0]]
        nodes_j = node_states[vertices[:, 1]]
        messages = _mlp3(jnp.concatenate([nodes_i, nodes_j, edges], axis=1), mW1, mb1, mW2, mb2, mW3, mb3)
        summed = jax.ops.segment_sum(messages, vertices[:, 0], num_segments=N) + jax.ops.segment_sum(messages, vertices[:, 1], num_segments=N)
        paired = node_states.reshape(-1, 2, NUM_NODES, D)
        attention = jnp.concatenate([paired[:, 0] - paired[:, 1], paired[:, 1] - paired[:, 0]], axis=1).reshape(-1, D)
        upd_in = jnp.concatenate([node_states, summed, attention], axis=1)
        return _mlp3(upd_in, uW1, ub1, uW2, ub2, uW3, ub3)
    edge_index_t = jnp.stack([src, dst], axis=1)
    x = _layernorm(x + _L0_gnn_ref(x, edge_attr_64, edge_index_t, L0_gnn_mW1, L0_gnn_mb1, L0_gnn_mW2, L0_gnn_mb2, L0_gnn_mW3, L0_gnn_mb3, L0_gnn_uW1, L0_gnn_ub1, L0_gnn_uW2, L0_gnn_ub2, L0_gnn_uW3, L0_gnn_ub3), axis=-1)
    return x

_drawn_inputs = setup_inputs


def setup_inputs(seed=0):
    import zlib

    import numpy as np

    out = dict(_drawn_inputs(seed))
    spreads = {'L0_gnn_mb1': (0.0, 0.8),
     'L0_gnn_mb2': (0.0, 0.612),
     'L0_gnn_mb3': (0.0, 0.429),
     'L0_gnn_ub1': (0.0, 2.0),
     'L0_gnn_ub2': (0.0, 1.476),
     'L0_gnn_ub3': (0.0, 0.301)}
    factors = {'edge_attr_64': 8.0, 'L0_gnn_mW1': 8.0, 'L0_gnn_mW2': 5.611, 'L0_gnn_mW3': 2.772}
    for name, (base, spread) in spreads.items():
        noise = np.random.default_rng([zlib.crc32(name.encode()), seed]).standard_normal(out[name].shape)
        drawn = base * np.exp(spread * noise) if base else spread * noise
        out[name] = jnp.asarray(drawn.astype(out[name].dtype))
    for name, factor in factors.items():
        out[name] = (out[name] * factor).astype(out[name].dtype)
    return out
```

```python
from contextlib import ExitStack

import concourse.bass as bass
from concourse import mybir

F32 = mybir.dt.float32
F32R = mybir.dt.float32r
I32 = mybir.dt.int32
I16 = mybir.dt.int16
U32 = mybir.dt.uint32
ALU = mybir.AluOpType
ACT = mybir.ActivationFunctionType
AX = mybir.AxisListType

P = 128
TILES = 4
CHUNK = TILES * P
EPS = 1e-5


def gnn_kernel(nc, x, src, dst, edge, mW1, mb1, mW2, mb2, mW3, mb3,
               uW1, ub1, uW2, ub2, uW3, ub3, out):
    N, D = x.shape
    E, ED = edge.shape
    H = mW2.shape[0]
    U = uW2.shape[0]
    NW = N // P
    NG = NW // TILES
    NQ = E // CHUNK
    NPAIR = E // (2 * P)
    NT = E // P
    R = max(r for r in range(2, P + 1, 2) if NPAIR % r == 0)
    G = NPAIR // R
    KH = H // P
    assert D == P and ED * 2 == P and H == 2 * P and U == 2 * P and NQ % 2 == 0 and NQ >= 6
    assert N % (2 * CHUNK) == 0

    p_table = nc.dram_tensor("p_table", (N, H), F32, kind="Internal").ap()
    rows16 = nc.dram_tensor("rows16", (2, E), I16, kind="Internal").ap()
    pair_stat = nc.dram_tensor("pair_stat", (2, NPAIR), F32, kind="Internal").ap()
    src_sum = [nc.dram_tensor(f"src_sum{t}", (N + P, D), F32, kind="Internal").ap() for t in range(TILES)]

    ctx = ExitStack()
    with ctx:
        def sb(name, shape, dt=F32):
            return ctx.enter_context(nc.sbuf_tensor(name, shape, dt))

        def sem(name):
            return ctx.enter_context(nc.semaphore(name))

        ctx.enter_context(nc.allow_non_contiguous_dma(reason="small tables"))

        x_sb = sb("x_sb", [P, NW, D])
        xT = sb("xT", [P, 2, CHUNK])
        q_hi = sb("q_hi", [P, NW, H], F32R)
        q_lo = sb("q_lo", [P, NW, H], F32R)
        acc = sb("acc", [P, NW, D])
        srcT = sb("srcT", [P, NT])
        dstT = sb("dstT", [P, NT])
        spareT = sb("spareT", [P, NT])
        node_row = sb("node_row", [P, N], I16)
        win_col = sb("win_col", [P, NW])
        ident = sb("ident", [P, P])
        before = sb("before", [P, P])
        spare_col = sb("spare_col", [P, 1])
        meta = sb("meta", [1, NQ, 4], I32)
        w1ab = sb("w1ab", [P, 2 * H])
        w1c = sb("w1c", [P, H])
        w1c_hi = sb("w1c_hi", [P, H], F32R)
        w1c_lo = sb("w1c_lo", [P, H], F32R)
        w2 = sb("w2", [P, KH, H])
        w3 = sb("w3", [P, KH, D])
        b1_all = sb("b1_all", [P, H])
        b2_col = sb("b2_col", [P, KH])
        b3_all = sb("b3_all", [P, D])
        uw1 = sb("uw1", [P, 3, U])
        uw2 = sb("uw2", [P, 2, U])
        uw3 = sb("uw3", [P, 2, D])
        ub1_col = sb("ub1_col", [P, 2])
        ub2_col = sb("ub2_col", [P, 2])
        ub3_all = sb("ub3_all", [P, D])

        pair_mm = sb("pair_mm", [R, 2, G])

        work_all = sb("work", [P, 15 * CHUNK])

        def work(start, size, rows=P):
            assert start + size <= 15 * CHUNK
            return work_all[0:rows, start:start + size]

        h1 = work(0, 2 * CHUNK).rearrange("p (t f) -> p t f", t=TILES)
        h1T = work(2 * CHUNK, 2 * CHUNK).rearrange("p (k e) -> p k e", k=KH)
        h2T = work(4 * CHUNK, 2 * CHUNK).rearrange("p (k e) -> p k e", k=KH)
        same_src = work(6 * CHUNK, 2 * CHUNK).rearrange("p (h t e) -> p h t e", h=2, t=TILES)
        hot_dst = work(8 * CHUNK, 2 * CHUNK).rearrange("p (h t n) -> p h t n", h=2, t=TILES)
        msg_sum = work(10 * CHUNK, 2 * CHUNK).rearrange("p (h t f) -> p h t f", h=2, t=TILES)
        msg = work(12 * CHUNK, CHUNK).rearrange("p (t f) -> p t f", t=TILES)
        e_split = work(13 * CHUNK, CHUNK).rearrange("p (t f) -> p t f", t=TILES)
        hot_dst_x = work(14 * CHUNK, CHUNK).rearrange("p (t n) -> p t n", t=TILES)
        e_raw = sb("e_raw", [P, 2, TILES, ED])
        rows = sb("rows", [P, 2, 2, CHUNK], I16)
        eT = sb("eT", [P, CHUNK], F32R)
        p_rows = sb("p_rows", [P, 2, TILES, H])
        hot_gather = sb("hot_gather", [P, TILES, P], F32R)
        hot_gather_x = sb("hot_gather_x", [P, TILES, P], F32R)
        scratch = sb("scratch", [P, TILES, P], mybir.dt.bfloat16)
        earlier = sb("earlier", [P, TILES])
        to_spare = sb("to_spare", [P, TILES])
        gather_idx = sb("gather_idx", [P, 2, TILES], U32)
        scatter_idx = sb("scatter_idx", [P, 2, TILES], U32)

        idx_i = work(0, 2 * G * 256, R).bitcast(I32)
        idx_f = work(2 * G * 256, 2 * G * 256, R).rearrange("r (a j) -> r a j", a=2)
        idx_s = work(4 * G * 256, G * 256, R).bitcast(I16).rearrange("r (a j) -> r a j", a=2)
        stat = work(0, 2 * NPAIR).rearrange("p (a q s) -> p a q s", a=2, s=2)
        bounds = work(2 * NPAIR, 2 * NQ).bitcast(I32).rearrange("p (a q) -> p a q", a=2)
        wins = work(2 * NPAIR + 2 * NQ, 2 * NQ).bitcast(I32).rearrange("p (a q) -> p a q", a=2)
        extra = work(2 * NPAIR + 4 * NQ, NQ)
        upto = [work(2 * NPAIR + (5 + i) * NQ, NQ) for i in range(2)]

        def bank(name):
            return ctx.enter_context(nc.psum_tensor(name, [P, CHUNK], F32))

        ps_e = bank("ps_e")
        ps_h1 = [bank("ps_h1a"), bank("ps_h1b")]
        ps_h2 = [bank("ps_h2a"), bank("ps_h2b")]
        ps_m = bank("ps_m")
        ps_s = bank("ps_s")
        ps_o = bank("ps_o")

        idx_loaded = sem("idx_loaded")
        x_loaded = sem("x_loaded")
        weights_loaded = sem("weights_loaded")
        consts = sem("consts")
        masks = sem("masks")
        idx_cast = sem("idx_cast")
        scratch_stored = sem("scratch_stored")
        stat_loaded = sem("stat_loaded")
        dve_chain = sem("dve_chain")
        act_chain = sem("act_chain")
        meta_ready = sem("meta_ready")
        idx_turned = sem("idx_turned")
        idxT_ready = sem("idxT_ready")
        x_turned = sem("x_turned")
        xT_ready = sem("xT_ready")
        pq_done = sem("pq_done")
        q_hi_done = sem("q_hi_done")
        pq_read = sem("pq_read")
        p_stored = [sem(f"p_stored{h}") for h in range(2)]
        aggregate_turn = sem("aggregate_turn")
        q_lo_done = sem("q_lo_done")
        w1c_hi_done = sem("w1c_hi_done")
        w1c_ready = sem("w1c_ready")
        zeros_ready = sem("zeros_ready")
        tables_zeroed = sem("tables_zeroed")
        e_loaded = [sem(f"e_loaded{h}") for h in range(2)]
        rows_loaded = [sem(f"rows_loaded{h}") for h in range(2)]
        gathered = [sem(f"gathered{h}") for h in range(2)]
        scattered = [sem(f"scattered{t}") for t in range(TILES)]
        gather_turn = sem("gather_turn")
        scatter_turn = sem("scatter_turn")
        e_hi_done = sem("e_hi_done")
        e_split_done = sem("e_split_done")
        e_turned = sem("e_turned")
        eT_ready = sem("eT_ready")
        gather_idx_ready = sem("gather_idx_ready")
        hot_gather_ready = sem("hot_gather_ready")
        h1_pre = sem("h1_pre")
        h1_ready = sem("h1_ready")
        h1_turned = sem("h1_turned")
        h1T_ready = sem("h1T_ready")
        h2_pre = sem("h2_pre")
        h2T_ready = sem("h2T_ready")
        m_pre = sem("m_pre")
        msg_ready = sem("msg_ready")
        same_ready = sem("same_ready")
        hot_ready = sem("hot_ready")
        counted = sem("counted")
        spare_found = sem("spare_found")
        scatter_idx_ready = sem("scatter_idx_ready")
        src_summed = sem("src_summed")
        msg_sum_ready = sem("msg_sum_ready")
        dst_summed = sem("dst_summed")
        acc_added = sem("acc_added")
        xg_ready = sem("xg_ready")
        xg_used = sem("xg_used")
        xs_ready = sem("xs_ready")
        xs_summed = sem("xs_summed")
        xs_added = sem("xs_added")
        tabs_loaded = sem("tabs_loaded")
        x_group_ready = sem("x_group_ready")
        x_group_turned = sem("x_group_turned")
        update_xT_ready = sem("update_xT_ready")
        y_chain = sem("y_chain")
        u_chain = sem("u_chain")
        node_sum_ready = sem("node_sum_ready")
        node_sum_turned = sem("node_sum_turned")
        sumT_ready = sem("sumT_ready")
        att_ready = sem("att_ready")
        u1_pre = sem("u1_pre")
        u1_ready = sem("u1_ready")
        u2_pre = sem("u2_pre")
        u2_ready = sem("u2_ready")
        u3_pre = sem("u3_pre")
        var_ready = sem("var_ready")
        std_ready = sem("std_ready")
        y_ready = sem("y_ready")
        out_stored = sem("out_stored")

        tabs = p_rows.rearrange("p a t h -> p (a t h)").rearrange("p (k w f) -> p k w f", k=TILES, f=D)
        sum_01, sum_23 = msg, hot_dst_x
        node_sum = msg_sum[:, 0]
        x_group = msg_sum[:, 1]
        sumT = work(0, CHUNK)
        attT = work(CHUNK, CHUNK)
        u1T, u2T = h1T, h2T
        y, y_norm = same_src[:, 0], same_src[:, 1]
        y_stats = hot_dst[:, 0, 0, 0:24].rearrange("p (t s) -> p t s", t=TILES)
        mean_var = hot_dst[:, 0, 1, 0:8].rearrange("p (t s) -> p t s", t=TILES)
        std = hot_dst[:, 0, 2, 0:TILES]
        rstd = hot_dst[:, 0, 3, 0:TILES]

        NWEIGHT = 15
        x_v = x.rearrange("(w p) f -> p w f", p=P)
        e_v = edge.rearrange("(pr p s) f -> p pr s f", p=P, s=2)
        out_v = out.rearrange("(w p) f -> p w f", p=P)
        p_v = p_table.rearrange("(w p) f -> p w f", p=P)
        tab_v = [t[0:N, :].rearrange("(w p) f -> p w f", p=P) for t in src_sum]

        def rows_view(h, which):
            return rows[:, h, which, :].rearrange("p (pr j s) -> p pr s j", pr=2, s=2)

        def by_pair(tile):
            return tile.rearrange("p (pr s) j -> p pr s j", s=2)

        def tile_cols(table, q):
            cols = table[:, bass.ds(q * TILES, TILES)].rearrange("p (pr s) -> p pr s", s=2)
            return cols.unsqueeze(3).to_broadcast([P, 2, 2, P])

        def later(n):
            return not (isinstance(n, int) and n == 0)

        def window(eng, q):
            return eng.value_load(meta[0:1, bass.ds(q, 1), 0:1].rearrange("a b c -> a (b c)"), min_val=0, max_val=NW - 1)

        def visits(eng, q):
            lo, hi = (eng.value_load(meta[0:1, bass.ds(q, 1), i:i + 1].rearrange("a b c -> a (b c)"),
                                     min_val=0, max_val=NQ * NW) for i in (1, 2))
            return lo, hi

        def extra_window(eng, w, k, lo):
            return nc.s_assert_within(eng.snap(w + 1 + k - lo), 0, NW - 1)

        block = ctx.enter_context(nc.Block())

        @block.sync
        def _(sp):
            sp.dma_start(idx_i[:, 0:G * 256].rearrange("r (g j) -> r g j", g=G),
                         src.rearrange("(g r j) -> r g j", r=R, j=256)).then_inc(idx_loaded, 16)
            sp.dma_start(idx_i[:, G * 256:].rearrange("r (g j) -> r g j", g=G),
                         dst.rearrange("(g r j) -> r g j", r=R, j=256)).then_inc(idx_loaded, 16)
            sp.dma_start(x_sb[:, :, :], x_v).then_inc(x_loaded, 16)
            weights = (
                (w1ab[:, 0:H], mW1[0:D, :]), (w1ab[:, H:2 * H], mW1[D:2 * D, :]),
                (w1c[0:ED, :], mW1[2 * D:, :]), (w1c[ED:P, :], mW1[2 * D:, :]),
                (b1_all[:, :], mb1.unsqueeze(0).to_broadcast([P, H])),
                (w2[:, :, :], mW2.rearrange("(k p) n -> p k n", p=P)),
                (w3[:, :, :], mW3.rearrange("(k p) n -> p k n", p=P)),
                (b2_col[:, :], mb2.rearrange("(k p) -> p k", p=P)),
                (b3_all[:, :], mb3.unsqueeze(0).to_broadcast([P, D])),
                (uw1[:, :, :], uW1.rearrange("(k p) n -> p k n", p=P)),
                (uw2[:, :, :], uW2.rearrange("(k p) n -> p k n", p=P)),
                (uw3[:, :, :], uW3.rearrange("(k p) n -> p k n", p=P)),
                (ub1_col[:, :], ub1.rearrange("(k p) -> p k", p=P)),
                (ub2_col[:, :], ub2.rearrange("(k p) -> p k", p=P)),
                (ub3_all[:, :], ub3.unsqueeze(0).to_broadcast([P, D])),
            )
            assert len(weights) == NWEIGHT
            for to, what in weights:
                sp.dma_start(to, what).then_inc(weights_loaded, 16)
            sp.wait_ge(idx_cast, 2)
            for a in range(2):
                sp.dma_start(rows16[a, :].rearrange("(g r j) -> r g j", r=R, j=256),
                             idx_s[:, a, :].rearrange("r (g j) -> r g j", g=G)).then_inc(scratch_stored, 16)
            sp.wait_ge(idx_cast, 4)
            for a in range(2):
                sp.dma_start(pair_stat[a, :].rearrange("(g r) -> r g", r=R), pair_mm[:, a, :]).then_inc(scratch_stored, 16)
            sp.wait_ge(scratch_stored, 64)
            sp.dma_start(work(0, 2 * NPAIR).rearrange("p (a q) -> p a q", a=2), pair_stat.unsqueeze(0).to_broadcast([P, 2, NPAIR])).then_inc(stat_loaded, 16)
            sp.wait_ge(zeros_ready, 1)
            for t in range(TILES):
                sp.dma_start(tab_v[t], acc[:, :, :]).then_inc(tables_zeroed, 16)
                sp.dma_start(src_sum[t][N:N + P, :], acc[:, 0, :]).then_inc(tables_zeroed, 16)

            def load_chunk(q, h, first):
                if not first:
                    sp.wait_ge(e_split_done, q - 1)
                sp.dma_start(e_raw[:, h, :, :].rearrange("p (pr s) f -> p pr (s f)", s=2),
                             e_v[:, bass.ds(q * 2, 2)].rearrange("p pr s f -> p pr (s f)")).then_inc(e_loaded[h], 16)
                if not first:
                    sp.wait_ge(hot_ready, q - 1)
                sp.dma_start(rows[:, h, :, :],
                             rows16[:, bass.ds(q * CHUNK, CHUNK)].unsqueeze(0).to_broadcast([P, 2, CHUNK])
                             ).then_inc(rows_loaded[h], 16)

            for h in range(2):
                load_chunk(h, h, True)
            with sp.Fori(0, NG // 2) as i:
                for h in range(2):
                    sp.wait_ge(pq_read, TILES * (2 * i + h + 1))
                    sp.dma_start(p_v[:, bass.ds((2 * i + h) * TILES, TILES), :], p_rows[:, h, :, :]).then_inc(p_stored[h], 16)
            with sp.Fori(1, NQ // 2) as b:
                for h in range(2):
                    load_chunk(2 * b + h, h, False)

            for t in range(TILES):
                sp.wait_ge(scattered[t], 16 * NQ)
            sp.wait_ge(h1_ready, 2 * NQ)

            def load_tabs(g):
                for t in range(TILES):
                    sp.dma_start(tabs[:, t, :, :], tab_v[t][:, bass.ds(g * TILES, TILES), :]).then_inc(tabs_loaded, 16)

            def store_out(g):
                sp.wait_ge(y_ready, g + 1)
                sp.dma_start(out_v[:, bass.ds(g * TILES, TILES), :], y_norm).then_inc(out_stored, 16)

            load_tabs(0)
            with sp.Fori(0, NG - 1) as g:
                sp.wait_ge(node_sum_ready, g + 1)
                load_tabs(g + 1)
                store_out(g)
            store_out(NG - 1)
            sp.wait_ge(out_stored, 16 * NG)

        @block.gpsimd
        def _(pool):
            pool.iota(node_row[:, :], [[1, N]], base=0, channel_multiplier=0,
                      allow_small_or_imprecise_dtypes=True).then_inc(consts, 1)
            pool.iota(win_col[:, :], [[P, NW]], base=0, channel_multiplier=1,
                      allow_small_or_imprecise_dtypes=True).then_inc(consts, 1)
            pool.iota(spare_col[:, :], [[1, 1]], base=N, channel_multiplier=1,
                      allow_small_or_imprecise_dtypes=True).then_inc(consts, 1)
            pool.memset(acc[:, :, :], 0.0).then_inc(zeros_ready, 1)

            def gather(q, h, first):
                if not first:
                    pool.wait_ge(h1_ready, 2 * q - 2)
                pool.wait_ge(gather_idx_ready, q + 1)
                pool.sem_inc(gather_turn, 1)
                for t in range(TILES):
                    pool.indirect_dma_start(
                        p_rows[:, h, t, :], None, p_table,
                        bass.IndirectOffsetOnAxis(ap=gather_idx[:, h, t:t + 1], axis=0)).then_inc(gathered[h], 16)

            def scatter(q, h):
                for t in range(TILES):
                    pool.wait_ge(scattered[t], 16 * q)
                pool.wait_ge(scatter_idx_ready, q + 1)
                pool.wait_ge(msg_sum_ready, q + 1)
                pool.sem_inc(scatter_turn, 1)
                for t in range(TILES):
                    pool.indirect_dma_start(
                        src_sum[t], bass.IndirectOffsetOnAxis(ap=scatter_idx[:, h, t:t + 1], axis=0),
                        msg_sum[:, h, t, :], None, compute_op=ALU.add).then_inc(scattered[t], 16)

            for h in range(2):
                pool.wait_ge(p_stored[h], 8 * NG)
            pool.wait_ge(tables_zeroed, 32 * TILES)
            gather(0, 0, True)
            gather(1, 1, True)
            gather(2, 0, False)
            gather(3, 1, False)
            scatter(0, 0)
            with pool.Fori(1, NQ // 2 - 1) as b:
                gather(2 * b + 2, 0, False)
                scatter(2 * b - 1, 1)
                gather(2 * b + 3, 1, False)
                scatter(2 * b, 0)
            scatter(NQ - 3, 1)
            scatter(NQ - 2, 0)
            scatter(NQ - 1, 1)

        @block.tensor
        def _(pe):
            pe.sem_inc(xg_used, 1)
            pe.sem_inc(xs_summed, 1)
            pe.wait_ge(idx_cast, 1)
            pe.wait_ge(masks, 1)
            banks = [ps_m, ps_s]
            n = 0
            for a in range(2):
                for g in range(G):
                    for s in range(2):
                        if n >= 2:
                            pe.wait_ge(idxT_ready, n - 1)
                        by_tile = idx_f[:, a, g * 256:(g + 1) * 256].rearrange("r (j s) -> r s j", s=2)
                        pe.transpose(banks[n % 2][:, 0:R], by_tile[:, s, :], ident[0:R, 0:R]).then_inc(idx_turned, 1)
                        n += 1
            pe.wait_ge(x_loaded, 16)
            pe.wait_ge(weights_loaded, 16 * NWEIGHT)

            def turn_x(g):
                if g >= 2:
                    pe.wait_ge(xT_ready, g - 1)
                for k in range(TILES):
                    last = pe.transpose(ps_h1[g % 2][:, k * P:(k + 1) * P], x_sb[:, g * TILES + k, :], ident[:, :])
                last.then_inc(x_turned, 1)

            turn_x(0)
            for g in range(NG):
                if g + 1 < NG:
                    turn_x(g + 1)
                pe.wait_ge(xT_ready, g + 1)
                for k in range(TILES):
                    w = g * TILES + k
                    if w >= 2:
                        pe.wait_ge(q_lo_done, w - 1)
                    pe.matmul(ps_h2[w % 2][:, :], xT[:, g % 2, k * P:(k + 1) * P], w1ab[:, :],
                              start=True, stop=True).then_inc(pq_done, 1)
            pe.wait_ge(q_lo_done, NW)
            pe.wait_ge(idxT_ready, 4 * G)
            pe.wait_ge(w1c_ready, 1)
            pe.wait_ge(meta_ready, 1)

            def turn_edges(q, first=False):
                pe.wait_ge(e_split_done, q + 1)
                if not first:
                    pe.wait_ge(eT_ready, q)
                for t in range(TILES):
                    last = pe.transpose(ps_e[:, t * P:(t + 1) * P], e_split[:, t, :], ident[:, :])
                last.then_inc(e_turned, 1)

            def layer1(q, first=False):
                w = window(pe, q)
                lo, hi = visits(pe, q)
                pe.wait_ge(eT_ready, q + 1)
                if not first:
                    pe.wait_ge(h1T_ready, 2 * q)
                for t in range(TILES):
                    at = ps_h1[t // 2][:, (t % 2) * H:(t % 2 + 1) * H]
                    for n, w1 in enumerate((w1c_hi, w1c_lo)):
                        pe.matmul(at, eT[:, t * P:(t + 1) * P], w1[:, :], start=(t % 2 == 0 and n == 0), stop=False,
                                  skip_group_check=True)
                pe.wait_ge(hot_gather_ready, q + 1)
                for t in range(TILES):
                    at = ps_h1[t // 2][:, (t % 2) * H:(t % 2 + 1) * H]
                    for table in (q_hi, q_lo):
                        last = pe.matmul(at, hot_gather[:, t, :],
                                         table[:, bass.ds(w, 1), :].rearrange("p a f -> p (a f)"),
                                         start=False, stop=True, skip_group_check=True)
                last.then_inc(h1_pre, 1)
                with pe.If(lo < hi):
                    with pe.Fori(lo, hi) as k:
                        wx = extra_window(pe, w, k, lo)
                        pe.wait_ge(xg_ready, k + 1)
                        for t in range(TILES):
                            at = ps_h1[t // 2][:, (t % 2) * H:(t % 2 + 1) * H]
                            for table in (q_hi, q_lo):
                                last = pe.matmul(at, hot_gather_x[:, t, :],
                                                 table[:, bass.ds(wx, 1), :].rearrange("p a f -> p (a f)"),
                                                 start=False, stop=True, skip_group_check=True)
                        last.then_inc(xg_used, 1)

            def turn_h1(q):
                pe.wait_ge(h1_ready, 2 * q + 1)
                for t in range(2):
                    pe.transpose(ps_h1[0][:, t * P:(t + 1) * P], h1[:, t, 0:P], ident[:, :])
                pe.wait_ge(h1_ready, 2 * q + 2)
                for t in range(2, TILES):
                    last = pe.transpose(ps_h1[0][:, t * P:(t + 1) * P], h1[:, t, 0:P], ident[:, :])
                last.then_inc(h1_turned, 1)
                for t in range(TILES):
                    last = pe.transpose(ps_h1[1][:, t * P:(t + 1) * P], h1[:, t, P:H], ident[:, :])
                last.then_inc(h1_turned, 1)

            def sum_messages(q, h, first):
                pe.wait_ge(msg_ready, q + 1)
                pe.wait_ge(hot_ready, q + 1)
                if not first:
                    pe.wait_ge(msg_sum_ready, q)
                for t in range(TILES):
                    last = pe.matmul(ps_s[:, t * D:(t + 1) * D], same_src[:, h, t, :], msg[:, t, :],
                                     start=True, stop=True)
                last.then_inc(src_summed, 1)
                if not first:
                    pe.wait_ge(acc_added, q)
                for t in range(TILES):
                    last = pe.matmul(ps_o[:, 0:D], hot_dst[:, h, t, :], msg[:, t, :],
                                     start=(t == 0), stop=(t == TILES - 1))
                last.then_inc(dst_summed, 1)
                lo, hi = visits(pe, q)
                with pe.If(lo < hi):
                    with pe.Fori(lo, hi) as k:
                        pe.wait_ge(xs_ready, k + 1)
                        pe.wait_ge(xs_added, k + 1)
                        for t in range(TILES):
                            last = pe.matmul(ps_o[:, 2 * D:3 * D], hot_dst_x[:, t, :], msg[:, t, :],
                                             start=(t == 0), stop=(t == TILES - 1))
                        last.then_inc(xs_summed, 1)

            def layer2(q, first=False):
                for m in range(KH):
                    pe.wait_ge(h1T_ready, 2 * q + KH)
                    if not first:
                        pe.wait_ge(h2T_ready, 2 * q - 1 + m)
                    for k in range(KH):
                        last = pe.matmul(ps_h2[m][:, :], w2[:, k, m * P:(m + 1) * P], h1T[:, k, :],
                                         start=(k == 0), stop=(k == KH - 1))
                    last.then_inc(h2_pre, 1)

            def layer3(q, first=False):
                pe.wait_ge(h2T_ready, 2 * q + 2)
                if not first:
                    pe.wait_ge(msg_ready, q)
                for t in range(TILES):
                    for k in range(KH):
                        last = pe.matmul(ps_m[:, t * D:(t + 1) * D], h2T[:, k, t * P:(t + 1) * P], w3[:, k, :],
                                         start=(k == 0), stop=(k == KH - 1))
                last.then_inc(m_pre, 1)

            def step(q, h, last=False):
                turn_h1(q)
                if not last:
                    turn_edges(q + 1)
                if later(q):
                    sum_messages(q - 1, 1 - h, isinstance(q, int) and q == 1)
                layer2(q, isinstance(q, int) and q == 0)
                if not last:
                    layer1(q + 1)
                layer3(q, isinstance(q, int) and q == 0)

            turn_edges(0, True)
            layer1(0, True)
            step(0, 0)
            step(1, 1)
            with pe.Fori(1, NQ // 2 - 1) as b:
                step(2 * b, 0)
                step(2 * b + 1, 1)
            step(NQ - 2, 0)
            step(NQ - 1, 1, last=True)
            sum_messages(NQ - 1, 1, False)

            pe.wait_ge(h1T_ready, 2 * NQ)
            pe.wait_ge(msg_sum_ready, NQ)
            pe.wait_ge(msg_ready, NQ)
            pe.wait_ge(acc_added, NQ)

            def update(g):
                pe.wait_ge(x_group_ready, g + 1)
                if later(g):
                    pe.wait_ge(update_xT_ready, g)
                for k in range(TILES):
                    last = pe.transpose(ps_e[:, k * P:(k + 1) * P], x_group[:, k, :], ident[:, :])
                last.then_inc(x_group_turned, 1)
                pe.wait_ge(node_sum_ready, g + 1)
                if later(g):
                    pe.wait_ge(sumT_ready, g)
                for k in range(TILES):
                    last = pe.transpose(ps_s[:, k * P:(k + 1) * P], node_sum[:, k, :], ident[:, :])
                last.then_inc(node_sum_turned, 1)
                pe.wait_ge(sumT_ready, g + 1)
                pe.wait_ge(att_ready, g + 1)
                if later(g):
                    pe.wait_ge(u1_ready, 2 * g)
                for m in range(2):
                    for k, part in enumerate((xT[:, 0, :], sumT, attT)):
                        last = pe.matmul(ps_h1[m][:, :], uw1[:, k, m * P:(m + 1) * P], part, start=(k == 0), stop=(k == 2))
                    last.then_inc(u1_pre, 1)
                pe.wait_ge(u1_ready, 2 * g + 2)
                if later(g):
                    pe.wait_ge(u2_ready, 2 * g)
                for m in range(2):
                    for k in range(2):
                        last = pe.matmul(ps_h2[m][:, :], uw2[:, k, m * P:(m + 1) * P], u1T[:, k, :], start=(k == 0), stop=(k == 1))
                    last.then_inc(u2_pre, 1)
                pe.wait_ge(u2_ready, 2 * g + 2)
                if later(g):
                    pe.wait_ge(y_ready, g)
                for t in range(TILES):
                    for k in range(2):
                        last = pe.matmul(ps_m[:, t * D:(t + 1) * D], u2T[:, k, t * P:(t + 1) * P], uw3[:, k, :],
                                         start=(k == 0), stop=(k == 1))
                last.then_inc(u3_pre, 1)

            update(0)
            with pe.Fori(1, NG) as g:
                update(g)

        @block.scalar
        def _(act):
            act.wait_ge(weights_loaded, 16 * NWEIGHT)
            act.activation(w1c_hi[:, :], w1c[:, :], ACT.Copy).then_inc(w1c_hi_done, 1)
            for g in range(NG):
                act.wait_ge(x_turned, g + 1)
                if g >= 2:
                    act.wait_ge(pq_done, TILES * (g - 1))
                act.activation(xT[:, g % 2, :], ps_h1[g % 2][:, :], ACT.Copy).then_inc(xT_ready, 1)
                for k in range(TILES):
                    w = g * TILES + k
                    act.wait_ge(pq_done, w + 1)
                    act.activation(q_hi[:, w, :], ps_h2[w % 2][:, H:2 * H], ACT.Copy).then_inc(q_hi_done, 1)

            def copy_eT(q, first=False):
                act.wait_ge(e_turned, q + 1)
                if not first:
                    act.wait_ge(h1_pre, q)
                act.activation(eT[:, :], ps_e[:, :], ACT.Copy).then_inc(eT_ready, 1)

            def relu_h1(q, first=False):
                for k in range(KH):
                    act.wait_ge(h1_turned, 2 * q + k + 1)
                    if not first and k == 0:
                        act.wait_ge(h2_pre, 2 * q)
                    act.activation(h1T[:, k, :], ps_h1[k][:, :], ACT.Relu).then_inc(h1T_ready, 1)

            def relu_h2(q, first=False):
                for m in range(KH):
                    act.wait_ge(h2_pre, 2 * q + m + 1)
                    if not first and m == 0:
                        act.wait_ge(m_pre, q)
                    act.activation(h2T[:, m, :], ps_h2[m][:, :], ACT.Relu, bias=b2_col[:, m:m + 1]).then_inc(h2T_ready, 1)

            def copy_msg_sum(q, h, first=False):
                act.wait_ge(src_summed, q + 1)
                if not first:
                    act.wait_ge(scatter_turn, q)
                act.activation(msg_sum[:, h, :, :], ps_s[:, :].rearrange("p (t f) -> p t f", t=TILES),
                               ACT.Copy).then_inc(msg_sum_ready, 1)

            def step(q, h, b, last=False):
                zero = isinstance(q, int) and q == 0
                relu_h1(q, zero)
                if not last:
                    copy_eT(q + 1)
                if not zero:
                    copy_msg_sum(q - 1, 1 - h, isinstance(q, int) and q <= 2)
                if not (last or (isinstance(q, int) and q >= NQ - 2)):
                    split_edges(q + 2, h, b + 1)
                relu_h2(q, zero)

            def split_edges(q, h, b):
                act.wait_ge(e_loaded[h], 16 * b + 16)
                if later(q):
                    act.wait_ge(e_turned, q)
                act.activation(e_split[:, :, 0:ED].bitcast(F32R), e_raw[:, h, :, :], ACT.Copy).then_inc(e_hi_done, 1)

            act.wait_ge(q_lo_done, NW)
            split_edges(0, 0, 0)
            copy_eT(0, True)
            split_edges(1, 1, 0)
            step(0, 0, 0)
            step(1, 1, 0)
            with act.Fori(1, NQ // 2 - 1) as b:
                step(2 * b, 0, b)
                step(2 * b + 1, 1, b)
            step(NQ - 2, 0, NQ // 2 - 1)
            step(NQ - 1, 1, NQ // 2 - 1, last=True)
            copy_msg_sum(NQ - 1, 1)

            for t in range(TILES):
                act.wait_ge(scattered[t], 16 * NQ)

            def update(g):
                if later(g):
                    act.wait_ge(x_group_turned, g)
                act.activation(x_group, x_sb[:, bass.ds(g * TILES, TILES), :], ACT.Copy).then_inc(x_group_ready, 1)
                act.wait_ge(x_group_turned, g + 1)
                if later(g):
                    act.wait_ge(u1_pre, 2 * g)
                    act.wait_ge(att_ready, g)
                act.activation(xT[:, 0, :], ps_e[:, :], ACT.Copy).then_inc(update_xT_ready, 1)
                act.wait_ge(node_sum_turned, g + 1)
                act.activation(sumT, ps_s[:, :], ACT.Copy).then_inc(sumT_ready, 1)
                for m in range(2):
                    act.wait_ge(u1_pre, 2 * g + m + 1)
                    if later(g):
                        act.wait_ge(u2_pre, 2 * g)
                    act.activation(u1T[:, m, :], ps_h1[m][:, :], ACT.Relu, bias=ub1_col[:, m:m + 1]).then_inc(u1_ready, 1)
                for m in range(2):
                    act.wait_ge(u2_pre, 2 * g + m + 1)
                    if later(g):
                        act.wait_ge(u3_pre, g)
                    act.activation(u2T[:, m, :], ps_h2[m][:, :], ACT.Relu, bias=ub2_col[:, m:m + 1]).then_inc(u2_ready, 1)
                act.wait_ge(var_ready, g + 1)
                act.activation(std, mean_var[:, :, 1], ACT.Sqrt).then_inc(std_ready, 1)

            update(0)
            with act.Fori(1, NG) as g:
                update(g)

        @block.vector
        def _(dve):
            chained = [0]

            def chain(ins):
                chained[0] += 1
                ins.then_inc(dve_chain, 1)
                dve.wait_ge(dve_chain, chained[0])

            dve.sem_inc(xs_added, 1)
            dve.wait_ge(idx_loaded, 32)
            dve.tensor_copy(idx_f, idx_i.rearrange("r (a j) -> r a j", a=2)).then_inc(idx_cast, 1)
            dve.tensor_copy(idx_s, idx_i.rearrange("r (a j) -> r a j", a=2)).then_inc(idx_cast, 1)
            dve.wait_ge(idx_cast, 2)
            by_pair_dst = idx_f[:, 1, :].rearrange("r (g j) -> r g j", g=G)
            dve.tensor_reduce(pair_mm[:, 0, :], by_pair_dst, AX.X, ALU.min).then_inc(idx_cast, 1)
            dve.tensor_reduce(pair_mm[:, 1, :], by_pair_dst, AX.X, ALU.max).then_inc(idx_cast, 1)
            dve.wait_ge(consts, 3)
            dve.tensor_scalar(ident[:, :], node_row[:, 0:P], win_col[:, 0:1], None, ALU.is_equal).then_inc(masks, 1)
            dve.tensor_scalar(before[:, :], node_row[:, 0:P], win_col[:, 0:1], None, ALU.is_lt).then_inc(masks, 1)
            dve.wait_ge(weights_loaded, 16 * NWEIGHT)
            dve.wait_ge(w1c_hi_done, 1)
            dve.tensor_tensor(w1c_lo[:, :], w1c[:, :], w1c_hi[:, :], ALU.subtract).then_inc(w1c_ready, 1)
            n = 0
            for a, table in enumerate((srcT, dstT)):
                for g in range(G):
                    for s in range(2):
                        dve.wait_ge(idx_turned, n + 1)
                        dve.tensor_copy(table[:, 2 * g * R:2 * (g + 1) * R].rearrange("p (r s) -> p s r", s=2)[:, s, :],
                                        (ps_m, ps_s)[n % 2][:, 0:R]).then_inc(idxT_ready, 1)
                        n += 1
            dve.wait_ge(stat_loaded, 16)
            dve.wait_ge(idxT_ready, 4 * G)
            dve.tensor_scalar(spareT[:, :], srcT[:, :], -1.0, spare_col[:, :], ALU.mult, ALU.add).then_inc(dve_chain, 1)
            chained[0] += 1
            dve.tensor_tensor(bounds[:, 0, :], stat[:, 0, :, 0], stat[:, 0, :, 1], ALU.min).then_inc(dve_chain, 1)
            chained[0] += 1
            chain(dve.tensor_tensor(bounds[:, 1, :], stat[:, 1, :, 0], stat[:, 1, :, 1], ALU.max))
            chain(dve.tensor_scalar(wins, bounds, 7, None, ALU.arith_shift_right))
            chain(dve.tensor_tensor(extra, wins[:, 1, :], wins[:, 0, :], ALU.subtract))
            chain(dve.tensor_copy(upto[0], extra))
            span, cur = 1, 0
            while span < NQ:
                dve.tensor_copy(upto[1 - cur][:, 0:span], upto[cur][:, 0:span]).then_inc(dve_chain, 1)
                chained[0] += 1
                chain(dve.tensor_tensor(upto[1 - cur][:, span:], upto[cur][:, span:], upto[cur][:, 0:NQ - span], ALU.add))
                span, cur = 2 * span, 1 - cur
            dve.tensor_copy(meta[:, :, 0], wins[0:1, 0, :]).then_inc(meta_ready, 1)
            dve.tensor_tensor(meta[:, :, 1], upto[cur][0:1, :], extra[0:1, :], ALU.subtract).then_inc(meta_ready, 1)
            dve.tensor_copy(meta[:, :, 2], upto[cur][0:1, :]).then_inc(meta_ready, 1)
            for w in range(NW):
                g, k = w // TILES, w % TILES
                dve.wait_ge(q_hi_done, w + 1)
                if g >= 2 and k == 0:
                    dve.wait_ge(p_stored[g % 2], 16 * (g // 2))
                dve.tensor_tensor(p_rows[:, g % 2, k, :], ps_h2[w % 2][:, 0:H], b1_all[:, :], ALU.add).then_inc(pq_read, 1)
                dve.tensor_tensor(q_lo[:, w, :], ps_h2[w % 2][:, H:2 * H], q_hi[:, w, :], ALU.subtract).then_inc(q_lo_done, 1)

            def pick_gather_idx(q, h, b):
                if b is not None:
                    dve.wait_ge(gathered[h], 16 * TILES * b)
                dve.tensor_copy(gather_idx[:, h, :], srcT[:, bass.ds(q * TILES, TILES)]).then_inc(gather_idx_ready, 1)

            def low_edges(q, h):
                dve.wait_ge(e_hi_done, q + 1)
                dve.tensor_tensor(e_split[:, :, ED:P], e_raw[:, h, :, :], e_split[:, :, 0:ED],
                                  ALU.subtract).then_inc(e_split_done, 1)

            def make_hot_gather(q, h, b, first=False):
                w = window(dve, q)
                dve.wait_ge(rows_loaded[h], 16 * b + 16)
                if not first:
                    dve.wait_ge(h1_pre, q)
                dve.tensor_scalar(by_pair(hot_gather[:, :, :]), rows_view(h, 1), win_col[:, bass.ds(w, 1)], None,
                                  ALU.is_equal).then_inc(hot_gather_ready, 1)

            def extra_hot_gather(q, h):
                w = window(dve, q)
                lo, hi = visits(dve, q)
                with dve.If(lo < hi):
                    with dve.Fori(lo, hi) as k:
                        wx = extra_window(dve, w, k, lo)
                        dve.wait_ge(xg_used, k + 1)
                        dve.tensor_scalar(by_pair(hot_gather_x[:, :, :]), rows_view(h, 1), win_col[:, bass.ds(wx, 1)],
                                          None, ALU.is_equal).then_inc(xg_ready, 1)
                dve.wait_ge(xg_used, hi + 1)

            def hot_rows(tile, q, w):
                nodes = node_row[:, bass.ds(w * P, P)]
                return dve.tensor_tensor(by_pair(tile), nodes.unsqueeze(1).unsqueeze(1).to_broadcast([P, 2, 2, P]),
                                         tile_cols(dstT, q), ALU.is_equal)

            def make_hot(q, h, first=False):
                w = window(dve, q)
                if not first:
                    dve.wait_ge(counted, q)
                    dve.wait_ge(dst_summed, q - 1)
                    dve.wait_ge(scatter_turn, q)
                dve.tensor_tensor(by_pair(same_src[:, h]), rows_view(h, 0), tile_cols(srcT, q), ALU.is_equal
                                  ).then_inc(same_ready, 1)
                for t in range(TILES):
                    view = rows[:, h, 0, :].rearrange("p (pr j s) -> p pr s j", pr=2, s=2)[:, t // 2, t % 2, :]
                    last = dve.scalar_tensor_tensor(scratch[:, t, :], view, srcT[:, bass.ds(q * TILES + t, 1)], before[:, :],
                                                    ALU.is_equal, ALU.mult, accum_out=earlier[:, t:t + 1])
                last.then_inc(counted, 1)
                hot_rows(hot_dst[:, h], q, w).then_inc(hot_ready, 1)
                dve.wait_ge(counted, q + 1)
                dve.scalar_tensor_tensor(to_spare[:, :], earlier[:, :], 0.0, spareT[:, bass.ds(q * TILES, TILES)],
                                         ALU.is_gt, ALU.mult).then_inc(spare_found, 1)
                dve.wait_ge(spare_found, q + 1)
                dve.tensor_tensor(scatter_idx[:, h, :], to_spare[:, :], srcT[:, bass.ds(q * TILES, TILES)],
                                  ALU.add).then_inc(scatter_idx_ready, 1)

            def add_to_acc(q):
                w = window(dve, q)
                lo, hi = visits(dve, q)
                if later(q):
                    dve.wait_ge(acc_added, q)
                    dve.wait_ge(xs_added, lo + 1)
                dve.wait_ge(dst_summed, q + 1)
                row = acc[:, bass.ds(w, 1), :].rearrange("p a f -> p (a f)")
                dve.tensor_tensor(row, row, ps_o[:, 0:D], ALU.add).then_inc(acc_added, 1)
                with dve.If(lo < hi):
                    with dve.Fori(lo, hi) as k:
                        wx = extra_window(dve, w, k, lo)
                        dve.wait_ge(xs_summed, k + 1)
                        hot_rows(hot_dst_x, q, wx).then_inc(xs_ready, 1)
                        dve.wait_ge(acc_added, q + 1)
                        dve.wait_ge(xs_added, k + 1)
                        dve.wait_ge(xs_summed, k + 2)
                        rowx = acc[:, bass.ds(wx, 1), :].rearrange("p a f -> p (a f)")
                        dve.tensor_tensor(rowx, rowx, ps_o[:, 2 * D:3 * D], ALU.add).then_inc(xs_added, 1)

            def add_h1(q, h, b, first=False):
                extra_hot_gather(q, h)
                dve.wait_ge(h1_pre, q + 1)
                dve.wait_ge(gathered[h], 16 * TILES * (b + 1))
                if not first:
                    dve.wait_ge(h1_turned, 2 * q)
                for j in range(2):
                    dve.tensor_tensor(h1[:, 2 * j:2 * j + 2, :], ps_h1[j][:, :].rearrange("p (t f) -> p t f", t=2),
                                      p_rows[:, h, 2 * j:2 * j + 2, :], ALU.add).then_inc(h1_ready, 1)

            def add_b3(q, first=False):
                dve.wait_ge(m_pre, q + 1)
                if not first:
                    dve.wait_ge(dst_summed, q)
                dve.tensor_tensor(msg, ps_m[:, :].rearrange("p (t f) -> p t f", t=TILES),
                                  b3_all[:, :].unsqueeze(1).to_broadcast([P, TILES, D]), ALU.add).then_inc(msg_ready, 1)

            def step(q, h, b, tail=0):
                zero = isinstance(q, int) and q == 0
                nb = b + 1 if h else b
                if tail < 1:
                    pick_gather_idx(q + 2, h, b + 1)
                if tail < 2:
                    make_hot_gather(q + 1, 1 - h, nb)
                make_hot(q, h, isinstance(q, int) and q < 2)
                if tail < 1:
                    low_edges(q + 2, h)
                if not zero:
                    add_to_acc(q - 1)
                if tail < 2:
                    add_h1(q + 1, 1 - h, nb)
                add_b3(q, zero)

            dve.wait_ge(meta_ready, 3)
            dve.wait_ge(tables_zeroed, 32 * TILES)
            for h in range(2):
                dve.wait_ge(p_stored[h], 8 * NG)
            pick_gather_idx(0, 0, None)
            pick_gather_idx(1, 1, None)
            make_hot_gather(0, 0, 0, True)
            low_edges(0, 0)
            low_edges(1, 1)
            add_h1(0, 0, 0, True)
            step(0, 0, 0)
            step(1, 1, 0)
            with dve.Fori(1, NQ // 2 - 1) as b:
                step(2 * b, 0, b)
                step(2 * b + 1, 1, b)
            step(NQ - 2, 0, NQ // 2 - 1, tail=1)
            step(NQ - 1, 1, NQ // 2 - 1, tail=2)
            add_to_acc(NQ - 1)

            def sum_nodes(g):
                dve.wait_ge(tabs_loaded, 16 * TILES * (g + 1))
                if later(g):
                    dve.wait_ge(node_sum_turned, g)
                dve.tensor_tensor(sum_01, tabs[:, 0], tabs[:, 1], ALU.add).then_inc(u_chain, 1)
                dve.tensor_tensor(sum_23, tabs[:, 2], tabs[:, 3], ALU.add).then_inc(u_chain, 1)
                dve.wait_ge(u_chain, 4 * g + 2)
                dve.tensor_tensor(sum_01, sum_01, sum_23, ALU.add).then_inc(u_chain, 1)
                dve.wait_ge(u_chain, 4 * g + 3)
                dve.tensor_tensor(node_sum, sum_01, acc[:, bass.ds(g * TILES, TILES), :], ALU.add).then_inc(node_sum_ready, 1)
                dve.wait_ge(node_sum_ready, g + 1)
                dve.sem_inc(u_chain, 1)

            def attention(g):
                dve.wait_ge(update_xT_ready, g + 1)
                if later(g):
                    dve.wait_ge(u1_pre, 2 * g)
                xw = xT[:, 0, :].rearrange("p (i s n) -> p i s n", s=2, n=P)
                aw = attT.rearrange("p (i s n) -> p i s n", s=2, n=P)
                dve.tensor_tensor(aw[:, :, 0, :], xw[:, :, 0, :], xw[:, :, 1, :], ALU.subtract)
                dve.tensor_tensor(aw[:, :, 1, :], xw[:, :, 1, :], xw[:, :, 0, :], ALU.subtract).then_inc(att_ready, 1)

            def normalize(g):
                dve.wait_ge(u3_pre, g + 1)
                dve.tensor_tensor(y, ps_m[:, :].rearrange("p (t f) -> p t f", t=TILES),
                                  x_sb[:, bass.ds(g * TILES, TILES), :], ALU.add).then_inc(y_chain, 1)
                dve.wait_ge(y_chain, 5 * g + 1)
                dve.tensor_tensor(y, y, ub3_all[:, :].unsqueeze(1).to_broadcast([P, TILES, D]), ALU.add).then_inc(y_chain, 1)
                dve.wait_ge(y_chain, 5 * g + 2)
                for t in range(TILES):
                    last = dve.bn_stats(y_stats[:, t, :], y[:, t, :])
                last.then_inc(y_chain, 1)
                dve.wait_ge(y_chain, 5 * g + 3)
                dve.sem_inc(aggregate_turn, 1)
                for t in range(TILES):
                    last = dve.bn_aggr(mean_var[:, t, :], y_stats[:, t, :])
                last.then_inc(y_chain, 1)
                dve.wait_ge(y_chain, 5 * g + 4)
                dve.tensor_scalar(mean_var[:, :, 1], mean_var[:, :, 1], EPS, None, ALU.add).then_inc(var_ready, 1)
                dve.wait_ge(std_ready, g + 1)
                dve.reciprocal(rstd, std).then_inc(y_chain, 1)
                dve.wait_ge(y_chain, 5 * g + 5)
                if later(g):
                    dve.wait_ge(out_stored, 16 * g)
                for t in range(TILES):
                    last = dve.tensor_scalar(y_norm[:, t, :], y[:, t, :], mean_var[:, t, 0:1], rstd[:, t:t + 1],
                                             ALU.subtract, ALU.mult)
                last.then_inc(y_ready, 1)

            dve.wait_ge(msg_sum_ready, NQ)
            for t in range(TILES):
                dve.wait_ge(scattered[t], 16 * NQ)
            def step_update(g):
                attention(g)
                sum_nodes(g + 1)
                normalize(g)

            sum_nodes(0)
            step_update(0)
            with dve.Fori(1, NG - 1) as g:
                step_update(g)
            attention(NG - 1)
            normalize(NG - 1)


_INS = ['x', 'src', 'dst', 'edge_attr_64', 'L0_gnn_mW1', 'L0_gnn_mb1', 'L0_gnn_mW2', 'L0_gnn_mb2', 'L0_gnn_mW3',
        'L0_gnn_mb3', 'L0_gnn_uW1', 'L0_gnn_ub1', 'L0_gnn_uW2', 'L0_gnn_ub2', 'L0_gnn_uW3', 'L0_gnn_ub3']


def kernel(**inputs):
    import numpy as _np
    import concourse.bacc as _bacc
    from concourse import mybir as _mybir
    from concourse.bass_utils import run_bass_kernel_spmd as _run

    nc = _bacc.Bacc("TRN2", target_bir_lowering=False, num_devices=1)
    arrays, args = {}, []
    for name in _INS:
        a = _np.ascontiguousarray(inputs[name])
        arrays[f"in_{name}_dram"] = a
        args.append(nc.dram_tensor(f"in_{name}_dram", a.shape, _mybir.dt.from_np(a.dtype), kind="ExternalInput").ap())
    shape = tuple(inputs['x'].shape)
    args.append(nc.dram_tensor("out_0_dram", shape, _mybir.dt.float32, kind="ExternalOutput").ap())
    gnn_kernel(nc, *args)
    r = _run(nc, [arrays], core_ids=[0])
    return r.results[0]["out_0_dram"]
```
